# Optimizing a Trainium2 kernel written in Bass

```python
import numpy as np
import jax
import jax.numpy as jnp

def _softmax(x, axis=-1):
    return jax.nn.softmax(x, axis=axis)
def _gelu(x):
    return jax.nn.gelu(x, approximate=True)
def _silu(x):
    return jax.nn.silu(x)
def _sigmoid(x):
    return jax.nn.sigmoid(x)
def _layernorm(x, axis=-1, eps=1e-5):
    m = jnp.mean(x, axis=axis, keepdims=True)
    v = jnp.var(x, axis=axis, keepdims=True)
    return (x - m) / jnp.sqrt(v + eps)
def _scatter_add(tgt, idx, src, axis=0):
    return tgt.at[idx].add(src)
def _segment_sum(src, seg, n):
    return jax.ops.segment_sum(src, seg, n)

kernel_name = 'mk_adj_resnorm_d2_adj_512_410fa4'

def setup_inputs(seed: int = 0):
    np.random.seed(seed)
    _w = jnp.asarray
    def _rec_inputs():
        import jax
        import jax.numpy as jnp
        _gk = jax.random.key(seed)
        x = -0.0002928 + 1 * jax.random.normal(jax.random.fold_in(_gk, 1), (16, 1024, 512), jnp.float32)
        _a = jax.random.bernoulli(jax.random.fold_in(_gk, 2), 0.00390625, (16, 1024, 1024))
        _a = jnp.logical_or(_a, jnp.swapaxes(_a, -1, -2))
        _a = jnp.logical_or(_a, jnp.eye(1024, dtype=bool))
        adj = _a.astype(jnp.int32)
        return x, adj
    x, adj = _rec_inputs()
    def _L0_gnn_setup():
        import jax, jax.numpy as jnp
        import numpy as np
        N_HEADS = 8
        N_HIDDEN = 64
        SLOPE = 0.2
        NEG = -9000000000000000.0
        key = jax.random.key(seed)
        k1, k2, k3, k4, k5 = jax.random.split(key, 5)
        B, N, F_in, F_out = (4, 2048, 512, 512)
        h = jax.random.normal(k1, (B, N, F_in), dtype=jnp.float32)
        adj = jax.random.randint(k2, (B, N, N), 0, 2, dtype=jnp.int32)
        lim_W = 1.414 * np.sqrt(6.0 / (F_in + F_out))
        W_l = jax.random.uniform(k3, (F_in, F_out), jnp.float32, -lim_W, lim_W)
        W_r = jax.random.uniform(k4, (F_in, F_out), jnp.float32, -lim_W, lim_W)
        lim_a = 1.414 * np.sqrt(6.0 / (N_HIDDEN + 1))
        a = jax.random.uniform(k5, (N_HIDDEN, 1), jnp.float32, -lim_a, lim_a)
        return {'h': h, 'adj': adj, 'W_l': W_l, 'W_r': W_r, 'a': a}
    _L0_gnn_all = _L0_gnn_setup()
    _L0_gnn_in = {k: v for k, v in _L0_gnn_all.items() if k in ('W_l', 'W_r', 'a', )}
    del _L0_gnn_all

    def _L1_gnn_setup():
        import jax, jax.numpy as jnp
        import numpy as np
        NEG_INF = -9000000000000000.0
        ALPHA = 0.2
        key = jax.random.key(seed)
        k1, k2, k3, k4, k5 = jax.random.split(key, 5)
        B, N, F_in, F_out, H = (4, 2048, 512, 64, 8)
        x = jax.random.normal(k1, (B, N, F_in), dtype=jnp.float32)
        adj = jax.random.randint(k2, (B, N, N), 0, 2, dtype=jnp.int32)
        W = jax.random.normal(k3, (H, F_in, F_out), dtype=jnp.float32) * (1.0 / np.sqrt(F_in))
        a1 = jax.random.normal(k4, (H, F_out), dtype=jnp.float32) * (1.0 / np.sqrt(2 * F_out))
        a2 = jax.random.normal(k5, (H, F_out), dtype=jnp.float32) * (1.0 / np.sqrt(2 * F_out))
        return {'x': x, 'adj': adj, 'W': W, 'a1': a1, 'a2': a2}
    _L1_gnn_all = _L1_gnn_setup()
    _L1_gnn_in = {k: v for k, v in _L1_gnn_all.items() if k in ('W', 'a1', 'a2', )}
    del _L1_gnn_all

    return {
        "x": x,
        "adj": adj,
        "L0_gnn_W_l": _L0_gnn_in["W_l"],
        "L0_gnn_W_r": _L0_gnn_in["W_r"],
        "L0_gnn_a": _L0_gnn_in["a"],
        "L1_gnn_W": _L1_gnn_in["W"],
        "L1_gnn_a1": _L1_gnn_in["a1"],
        "L1_gnn_a2": _L1_gnn_in["a2"],
    }

def reference(x, adj, L0_gnn_W_l, L0_gnn_W_r, L0_gnn_a, L1_gnn_W, L1_gnn_a1, L1_gnn_a2):
    import jax
    import jax.numpy as jnp
    def _L0_gnn_ref(h, adj, W_l, W_r, a):
        import jax, jax.numpy as jnp
        import numpy as np
        N_HEADS = 8
        N_HIDDEN = 64
        SLOPE = 0.2
        NEG = -9000000000000000.0
        B, N, _ = h.shape
        H, d = (N_HEADS, N_HIDDEN)
        Wh_l = jax.nn.leaky_relu((h @ W_l).reshape(B, H, N, d), SLOPE)
        Wh_r = jax.nn.leaky_relu((h @ W_r).reshape(B, H, N, d), SLOPE)
        e = Wh_l @ a + jnp.swapaxes(Wh_r @ a, 2, 3)
        att = jnp.where(adj[:, None, :, :] > 0, e, NEG)
        att = jax.nn.softmax(att, axis=-1)
        h_prime = att @ Wh_r
        out = jax.nn.elu(h_prime.reshape(B, N, H * d))
        return out

    def _L1_gnn_ref(x, adj, W, a1, a2):
        import jax, jax.numpy as jnp
        import numpy as np
        NEG_INF = -9000000000000000.0
        ALPHA = 0.2
        h = jnp.einsum('bnf,hfo->bhno', x, W)
        s1 = jnp.einsum('bhno,ho->bhn', h, a1)
        s2 = jnp.einsum('bhno,ho->bhn', h, a2)
        e = jax.nn.leaky_relu(s1[..., :, None] + s2[..., None, :], negative_slope=ALPHA)
        mask = (adj > 0)[:, None, :, :]
        attn = jax.nn.softmax(jnp.where(mask, e, NEG_INF), axis=-1)
        h_prime = jnp.einsum('bhnm,bhmo->bhno', attn, h)
        B, H, N, Fo = h_prime.shape
        return jnp.transpose(h_prime, (0, 2, 1, 3)).reshape(B, N, H * Fo)

    x = _layernorm(x + _L0_gnn_ref(x, adj, L0_gnn_W_l, L0_gnn_W_r, L0_gnn_a), axis=-1)
    x = _layernorm(x + _L1_gnn_ref(x, adj, L1_gnn_W, L1_gnn_a1, L1_gnn_a2), axis=-1)
    return x


_drawn_inputs = setup_inputs


def setup_inputs(seed=0):
    import zlib

    import numpy as np

    out = dict(_drawn_inputs(seed))
    spreads = {}
    factors = {}
    for name, (base, spread) in spreads.items():
        noise = np.random.default_rng([zlib.crc32(name.encode()), seed]).standard_normal(out[name].shape)
        drawn = base * np.exp(spread * noise) if base else spread * noise
        out[name] = jnp.asarray(drawn.astype(out[name].dtype))
    for name, factor in factors.items():
        out[name] = (out[name] * factor).astype(out[name].dtype)
    return out
```

```python
from contextlib import ExitStack

import concourse.bass as bass
from concourse import mybir

ALU = mybir.AluOpType
ACT = mybir.ActivationFunctionType
AX = mybir.AxisListType
F32 = mybir.dt.float32
F32R = mybir.dt.float32r
BF16 = mybir.dt.bfloat16
I32 = mybir.dt.int32
U8 = mybir.dt.uint8

P = 128
SLOPE = 0.2
EPS = 1e-5


def need(eng, sem, count):
    if isinstance(count, int) and count <= 0:
        return
    eng.wait_ge(sem, count)


def need_first(eng, sem, count, passed):
    if isinstance(count, int) and count <= 0:
        return
    eng.wait_ge(sem, count)
    eng.sem_inc(passed, 1)


def layer0(nc, x, adj, W_r, a, x1_d, at_d, B):
    N, D = x.shape[1], x.shape[2]
    T = N // P
    KC = D // P
    H, d = T, D // T
    TA = 4
    R = 6
    C = d + 1
    Q = H // 2
    assert N // T == P and H * d == D

    with ExitStack() as ctx:
        sb = lambda name, shape, dt: ctx.enter_context(nc.sbuf_tensor("l0_" + name, shape, dt))
        ps = lambda name, shape, dt: ctx.enter_context(nc.psum_tensor("l0_" + name, shape, dt))
        sem = lambda name: ctx.enter_context(nc.semaphore("l0_" + name))

        adj_in = [sb(f"adj_in{i}", [P, N], I32) for i in range(4)]
        adj_bf = [sb(f"adj_bf{i}", [P, N], BF16) for i in range(2)]
        at_build = [sb(f"at_build{i}", [P, T, N // 2], U8) for i in range(2)]
        at_use = sb("at_use", [P, T, N], U8)
        at_tile = [sb(f"at_tile{i}", [P, T, P], F32R) for i in range(2)]
        x_all = sb("x_all", [P, T, D], F32)
        rows = [sb(f"rows{i}", [P, D], F32) for i in range(R)]
        xT_hi = [sb(f"xT_hi{i}", [P, KC, P], F32R) for i in range(2)]
        xT_lo = [sb(f"xT_lo{i}", [P, KC, P], F32R) for i in range(2)]
        w_hi = sb("w_hi", [P, KC, D], F32R)
        w_lo = sb("w_lo", [P, KC, D], F32R)
        wh = sb("wh", [P, H, T, C], F32)
        a_bc = sb("a_bc", [P, d], F32)
        wh_a = [sb(f"wh_a{i}", [P, T, d], F32) for i in range(2)]
        fr = sb("fr", [P, H, T], F32)
        fr_max = sb("fr_max", [P, H], F32)
        fr_top = sb("fr_top", [P, H], F32)
        fr_sh = sb("fr_sh", [P, H, T], F32)
        p_exp = sb("p_exp", [P, H, T], F32)
        xw = [sb(f"xw{i}", [P, T, C], F32) for i in range(2)]
        xs = [sb(f"xs{i}", [P, T, 2, H, C], F32R) for i in range(2)]
        rden = [sb(f"rden{i}", [P, 2, Q], F32) for i in range(2)]
        hp = sb("hp", [P, H, T, d], F32)
        neg = [sb(f"neg{i}", [P, D], F32) for i in range(2)]
        stats = [sb(f"stats{i}", [P, 6], F32) for i in range(2)]
        mv = [sb(f"mv{i}", [P, 2], F32) for i in range(3)]
        rstd = [sb(f"rstd{i}", [P, 1], F32) for i in range(3)]
        mhalf = sb("mhalf", [P, 1], F32)
        ident = sb("ident", [P, P], F32)
        ident_bf = sb("ident_bf", [P, P], BF16)
        w_raw = x_all[:, 0:KC, :]

        ps_at = ps("ps_at", [P, T, P], BF16)
        ps_xt = ps("ps_xt", [P, KC, P], F32)
        ps_y = [ps(f"ps_y{i}", [P, D], F32) for i in range(2)]
        ps_agg = [ps(f"ps_agg{i}", [P, 2, 512], F32) for i in range(2)]

        w_loaded = sem("w_loaded")
        w_hi_ready = sem("w_hi_ready")
        w_ready = sem("w_ready")
        a_loaded = sem("a_loaded")
        const_ready = sem("const_ready")
        ident_ready = sem("ident_ready")
        sp_passed = sem("sp_passed")
        pool_passed = sem("pool_passed")
        dve_passed = sem("dve_passed")
        adj_loaded = [sem(f"adj_loaded{i}") for i in range(4)]
        adj_cast = sem("adj_cast")
        at_turned = sem("at_turned")
        at_built = sem("at_built")
        at_stored = sem("at_stored")
        at_loaded = sem("at_loaded")
        at_tile_ready = sem("at_tile_ready")
        x_loaded = sem("x_loaded")
        x_res_loaded = [sem(f"x_res_loaded{i}") for i in range(R)]
        x_turned = sem("x_turned")
        xT_hi_ready = sem("xT_hi_ready")
        xT_lo_ready = sem("xT_lo_ready")
        projected = sem("projected")
        wh_out = sem("wh_out")
        wh_ready = sem("wh_ready")
        wh_a_ready = sem("wh_a_ready")
        fr_ready = sem("fr_ready")
        fr_max_ready = sem("fr_max_ready")
        fr_top_ready = sem("fr_top_ready")
        fr_sh_ready = sem("fr_sh_ready")
        p_ready = sem("p_ready")
        xw_ready = sem("xw_ready")
        xs_hi_ready = sem("xs_hi_ready")
        xs_ready = sem("xs_ready")
        aggregated = sem("aggregated")
        rden_ready = sem("rden_ready")
        hp_ready = sem("hp_ready")
        neg_ready = sem("neg_ready")
        neg_exp = sem("neg_exp")
        y_ready = sem("y_ready")
        y2_ready = sem("y2_ready")
        stats_ready = sem("stats_ready")
        mv_ready = sem("mv_ready")
        var_ready = sem("var_ready")
        rstd_ready = sem("rstd_ready")
        x1_ready = sem("x1_ready")
        x1_stored = [sem(f"x1_stored{i}") for i in range(R)]

        ORDER = [(w[0], int(w[1:])) for w in (
            "P0 V0 t0 L0 L1 P1 A0 L2 t1 L3 P2 A1 L4 L5 P3 L6 L7 t2 P4 L8 P5 E0 P6 A2 E1 L9 t3 P7 A3 E2 t4 P8 M0 A4 "
            "t5 E3 X0 X1 A5 t6 E4 X2 X3 A6 t7 E5 X4 X5 A7 E6 X6 X7 E7").split()]

        def walk(eng, parts):
            def step(s, par, stages):
                for kind, k in ORDER:
                    if kind in parts and {"E": "A", "V": "A", "t": "A", "M": "P", "X": "P"}.get(kind, kind) in stages:
                        parts[kind](s, par, k)
            step(0, 0, "P")
            step(1, 1, "PA")
            step(2, 0, "PAL")
            step(3, 1, "PAL")
            with eng.Fori(2, B // 2) as i:
                step(2 * i, 0, "PAL")
                step(2 * i + 1, 1, "PAL")
            step(B, 0, "AL")
            step(B + 1, 1, "L")

        block = ctx.enter_context(nc.Block())

        @block.sync
        def _(sp):
            sp.dma_start(w_raw, W_r.rearrange("(k p) n -> p k n", p=P)).then_inc(w_loaded, 16)
            sp.dma_start(a_bc[:, :], a.rearrange("d o -> o d").broadcast_to([P, d])).then_inc(a_loaded, 16)

            def load(s, par, t):
                if t == 0:
                    need_first(sp, w_ready, 1, sp_passed)
                    need_first(sp, x_turned, s * T, sp_passed)
                    sp.dma_start(x_all[:, :, :], x[bass.ds(s, 1)].rearrange("a (t p) f -> p (a t) f", p=P)
                                 ).then_inc(x_loaded, 16)
                for r in range(TA) if t == 0 else [t + 3] if t + 3 < T else []:
                    need_first(sp, adj_cast, s * T + r - 3, sp_passed)
                    sp.dma_start(adj_in[r % TA][:, :], adj[bass.ds(s, 1), r * P:(r + 1) * P, :].rearrange("a p n -> (a p) n")
                                 ).then_inc(adj_loaded[r % TA], 16)
                if t == T // 2 or t == T:
                    half = t // (T // 2) - 1
                    need_first(sp, at_built, s * T + t, sp_passed)
                    sp.dma_start(at_d[bass.ds(s, 1), :, half * N // 2:(half + 1) * N // 2].rearrange(
                        "a (t p) n -> p (a t) n", p=P), at_build[half][:, :, :]).then_inc(at_stored, 16)

            def load_at(s, par, _):
                b = s - 1
                need_first(sp, at_stored, (b + 1) * 32, sp_passed)
                need_first(sp, at_tile_ready, b * T, sp_passed)
                sp.dma_start(at_use[:, :, :], at_d[bass.ds(b, 1)].rearrange("a (r c) n -> r (a c) n", c=T)
                             ).then_inc(at_loaded, 16)

            def uses(b, k):
                return b * len(range(k % R, T, R)) + k // R

            def store(s, par, k):
                b = s - 2
                for j in range(3) if k == 0 else [k + 2] if k + 2 < T else []:
                    need_first(sp, x1_stored[j % R], 16 * uses(b, j), sp_passed)
                    sp.dma_start(rows[j % R][:, :], x[bass.ds(b, 1), j * P:(j + 1) * P, :].rearrange("a p f -> (a p) f")
                                 ).then_inc(x_res_loaded[j % R], 16)
                if k >= 2:
                    h = k - 2
                    need_first(sp, x1_ready, b * T + h + 1, sp_passed)
                    sp.dma_start(x1_d[bass.ds(b, 1), h * P:(h + 1) * P, :].rearrange("a p f -> (a p) f"),
                                 rows[h % R][:, :]).then_inc(x1_stored[h % R], 16)

            walk(sp, {"P": load, "V": load_at, "L": store})
            for i in range(R):
                sp.wait_ge(x1_stored[i], 16 * B * len(range(i, T, R)))

        @block.gpsimd
        def _(pool):
            pool.memset(ident[:, :], 0.0).then_inc(ident_ready, 1)
            pool.memset(ident_bf[:, :], 0.0).then_inc(ident_ready, 1)
            pool.memset(mhalf[:, :], -0.5).then_inc(const_ready, 1)
            pool.memset(wh[:, :, :, d:C], 1.0).then_inc(const_ready, 1)
            pool.wait_ge(ident_ready, 2)
            for m in (ident, ident_bf):
                pool.affine_select(out=m[:, :], in_=m[:, :], compare_op=ALU.not_equal, fill=1.0, base=0,
                                   pattern=[[-1, P]], channel_multiplier=1).then_inc(ident_ready, 1)
            pool.wait_ge(a_loaded, 16)

            def project(s, par, t):
                for j in [t - 2] if 2 <= t < T else [t - 2, t - 1] if t == T else []:
                    need(pool, wh_ready, s * T + j + 1)
                    need(pool, fr_ready, s * T + j - 1)
                    pool.tensor_tensor(wh_a[j % 2][:, :, :], wh[:, j, :, 0:d],
                                       a_bc[:, :].unsqueeze(1).broadcast_to([P, T, d]), ALU.mult
                                       ).then_inc(wh_a_ready, 1)

            def top(s, par, _):
                need_first(pool, fr_max_ready, s + 1, pool_passed)
                pool.partition_all_reduce(fr_top[:, :], fr_max[:, :], P, bass.bass_isa.ReduceOp.max
                                          ).then_inc(fr_top_ready, 1)

            def tiles(s, par, k):
                b = s - 1
                if k == 0:
                    need_first(pool, at_loaded, (b + 1) * 16, pool_passed)
                for c in [0, 1] if k == 0 else [k + 1] if k + 1 < T else []:
                    need_first(pool, aggregated, b * T + c - 1, pool_passed)
                    pool.tensor_scalar(at_tile[c % 2][:, :, :], at_use[:, :, c:N:T], 1.0, 0.0,
                                       ALU.mult, ALU.add).then_inc(at_tile_ready, 1)

            def norm(s, par, k):
                if 1 <= k <= T:
                    h = k - 1
                    n = (s - 2) * T + h + 1
                    need_first(pool, mv_ready, n, pool_passed)
                    pool.tensor_scalar(mv[h % 3][:, 1:2], mv[h % 3][:, 1:2], EPS, 1.0, ALU.add, ALU.mult).then_inc(var_ready, 1)
                    need(pool, var_ready, n)
                    pool.tensor_tensor(rstd[h % 3][:, :], mv[h % 3][:, 1:2], mhalf[:, :], ALU.pow
                                       ).then_inc(rstd_ready, 1)

            walk(pool, {"P": project, "M": top, "t": tiles, "L": norm})

        @block.scalar
        def _(act):
            act.wait_ge(w_loaded, 16)
            act.activation(w_hi[:, :, :], w_raw, ACT.Copy).then_inc(w_hi_ready, 1)
            act.wait_ge(const_ready, 2)

            def project(s, par, t):
                n = s * T + t
                if t < T:
                    need(act, x_turned, n + 1)
                    need(act, projected, n - 1)
                    act.activation(xT_hi[t % 2][:, :, :], ps_xt[:, :, :], ACT.Copy).then_inc(xT_hi_ready, 1)
                    if t % (T // 2) == 0:
                        need(act, at_stored, s * 32 + (t // (T // 2) - 1) * 16)
                    need(act, at_turned, n + 1)
                    o = t % (T // 2) * P
                    act.activation(at_build[t // (T // 2)][:, :, o:o + P], ps_at[:, :, :], ACT.Copy).then_inc(at_built, 1)
                if t >= 1:
                    j = t - 1
                    m = s * T + j
                    need(act, projected, m + 1)
                    if j == 0:
                        need(act, xw_ready, s * T)
                    act.activation(wh[:, j, :, 0:d], ps_y[j % 2][:, :].rearrange("p (c d) -> p c d", c=T),
                                   ACT.Copy).then_inc(wh_out, 1)

            def weights(s, par, _):
                need(act, fr_sh_ready, s + 1)
                act.activation(p_exp[:, :, :], fr_sh[:, :, :], ACT.Exp).then_inc(p_ready, 1)

            def split(s, par, h):
                need(act, xw_ready, s * T + h + 1)
                if h == 0:
                    need(act, aggregated, (s - 1) * T)
                act.activation(xs[par][:, :, 0, h, :], xw[h % 2][:, :, :], ACT.Copy).then_inc(xs_hi_ready, 1)

            def norm(s, par, k):
                if k < T:
                    n = (s - 2) * T + k
                    need(act, neg_ready, n + 1)
                    act.activation(neg[k % 2][:, :], neg[k % 2][:, :], ACT.Exp).then_inc(neg_exp, 1)

            walk(act, {"P": project, "M": weights, "X": split, "L": norm})

        @block.vector
        def _(dve):
            dve.wait_ge(w_hi_ready, 1)
            dve.tensor_tensor(w_lo[:, :, :], w_raw, w_hi[:, :, :].bitcast(F32), ALU.subtract).then_inc(w_ready, 1)

            def cast(s, t):
                need(dve, adj_loaded[t % TA], (s * (T // TA) + t // TA + 1) * 16)
                need(dve, at_turned, s * T + t - 1)
                dve.tensor_scalar(adj_bf[t % 2][:, :], adj_in[t % TA][:, :], 0, None, ALU.is_gt).then_inc(adj_cast, 1)

            def leaky(s, j):
                need(dve, wh_out, s * T + j + 1)
                dve.scalar_tensor_tensor(out=wh[:, j, :, 0:d], in0=wh[:, j, :, 0:d], scalar=SLOPE,
                                         in1=wh[:, j, :, 0:d], op0=ALU.mult, op1=ALU.max).then_inc(wh_ready, 1)

            def project(s, par, t):
                n = s * T + t
                if t == 0:
                    cast(s, 0)
                if t < T - 1:
                    cast(s, t + 1)
                if t < T:
                    need(dve, xT_hi_ready, n + 1)
                    need(dve, projected, n - 1)
                    dve.tensor_tensor(xT_lo[t % 2][:, :, :], ps_xt[:, :, :], xT_hi[t % 2][:, :, :].bitcast(F32),
                                      ALU.subtract).then_inc(xT_lo_ready, 1)
                if t >= 2:
                    leaky(s, t - 2)
                if t >= 3:
                    score(s, t - 3)
                if t == T:
                    leaky(s, T - 1)
                    score(s, T - 2)
                    score(s, T - 1)

            def score(s, j):
                need(dve, wh_a_ready, s * T + j + 1)
                dve.tensor_reduce(fr[:, j, :], wh_a[j % 2][:, :, :], AX.X, ALU.add).then_inc(fr_ready, 1)

            def top(s, par, _):
                need(dve, fr_ready, (s + 1) * T)
                dve.tensor_reduce(fr_max[:, :], fr[:, :, :], AX.X, ALU.max).then_inc(fr_max_ready, 1)
                need(dve, fr_top_ready, s + 1)
                dve.tensor_tensor(fr_sh[:, :, :], fr[:, :, :], fr_top[:, :].unsqueeze(2).broadcast_to([P, H, T]),
                                  ALU.subtract).then_inc(fr_sh_ready, 1)

            def split(s, par, h):
                n = s * T + h
                if h == 0:
                    need(dve, p_ready, s + 1)
                need(dve, xs_ready, n - 1)
                dve.tensor_tensor(xw[h % 2][:, :, :], wh[:, h, :, :],
                                  p_exp[:, h, :].unsqueeze(2).broadcast_to([P, T, C]), ALU.mult).then_inc(xw_ready, 1)
                need(dve, xs_hi_ready, n + 1)
                dve.tensor_tensor(xs[par][:, :, 1, h, :], xw[h % 2][:, :, :], xs[par][:, :, 0, h, :].bitcast(F32),
                                  ALU.subtract).then_inc(xs_ready, 1)

            def aggregate(s, par, c):
                n = (s - 1) * T + c
                if c == 0:
                    need(dve, neg_ready, (s - 1) * T)
                    need(dve, y_ready, (s - 1) * T)
                need(dve, aggregated, n + 1)
                dve.reciprocal(rden[c % 2][:, :, :], ps_agg[c % 2][:, :, d:Q * C:C]).then_inc(rden_ready, 1)
                need(dve, rden_ready, n + 1)
                dve.tensor_tensor(hp[:, :, c, :].rearrange("p (g q) d -> p g q d", g=2),
                                  ps_agg[c % 2][:, :, 0:Q * C].rearrange("p g (q c) -> p g q c", q=Q)[:, :, :, 0:d],
                                  rden[c % 2][:, :, :].unsqueeze(3).broadcast_to([P, 2, Q, d]), ALU.mult
                                  ).then_inc(hp_ready, 1)

            def norm(s, par, k):
                b = s - 2
                if k < T:
                    n = b * T + k
                    z = hp[:, k, :, :].rearrange("p c d -> p (c d)")
                    if k == 0:
                        need(dve, hp_ready, (b + 1) * T)
                    dve.tensor_scalar(neg[k % 2][:, :], z, 0.0, None, ALU.min).then_inc(neg_ready, 1)
                    need(dve, x_res_loaded[k % R], 16 * (b * len(range(k % R, T, R)) + k // R + 1))
                    dve.scalar_tensor_tensor(out=rows[k % R][:, :], in0=z, scalar=0.0, in1=rows[k % R][:, :],
                                             op0=ALU.max, op1=ALU.add).then_inc(y_ready, 1)
                if 1 <= k <= T:
                    j = k - 1
                    n = b * T + j + 1
                    need(dve, neg_exp, n)
                    need(dve, y_ready, n)
                    dve.scalar_tensor_tensor(out=rows[j % R][:, :], in0=neg[j % 2][:, :], scalar=-1.0, in1=rows[j % R][:, :],
                                             op0=ALU.add, op1=ALU.add).then_inc(y2_ready, 1)
                    need(dve, y2_ready, n)
                    dve.bn_stats(stats[j % 2][:, :], rows[j % R][:, :]).then_inc(stats_ready, 1)
                    need_first(dve, stats_ready, n, dve_passed)
                    dve.bn_aggr(mv[j % 3][:, :], stats[j % 2][:, :]).then_inc(mv_ready, 1)
                if k >= 2:
                    j = k - 2
                    need(dve, rstd_ready, b * T + j + 1)
                    dve.tensor_scalar(rows[j % R][:, :], rows[j % R][:, :], mv[j % 3][:, 0:1], rstd[j % 3][:, 0:1],
                                      ALU.subtract, ALU.mult).then_inc(x1_ready, 1)

            walk(dve, {"P": project, "M": top, "X": split, "E": aggregate, "L": norm})

        @block.tensor
        def _(pe):
            pe.wait_ge(ident_ready, 4)
            pe.wait_ge(w_ready, 1)

            def project(s, par, t):
                n = s * T + t
                if t < T:
                    if t == 0:
                        need(pe, x_loaded, (s + 1) * 16)
                    need(pe, xT_lo_ready, n)
                    for k in range(KC):
                        mm = pe.transpose(ps_xt[:, k, :], x_all[:, t, k * P:(k + 1) * P], ident[:, :])
                    mm.then_inc(x_turned, 1)
                    need(pe, adj_cast, n + 1)
                    need(pe, at_built, n)
                    for u in range(T):
                        mm = pe.transpose(ps_at[:, u, :], adj_bf[t % 2][:, u * P:(u + 1) * P], ident_bf[:, :])
                    mm.then_inc(at_turned, 1)
                if t >= 1:
                    j = t - 1
                    m = s * T + j
                    need(pe, xT_lo_ready, m + 1)
                    need(pe, wh_out, m - 1)
                    for k in range(KC):
                        pe.matmul(ps_y[j % 2][:, :], xT_hi[j % 2][:, k, :], w_hi[:, k, :], start=(k == 0), stop=False)
                        pe.matmul(ps_y[j % 2][:, :], xT_hi[j % 2][:, k, :], w_lo[:, k, :], start=False, stop=False)
                        mm = pe.matmul(ps_y[j % 2][:, :], xT_lo[j % 2][:, k, :], w_hi[:, k, :], start=False,
                                       stop=(k == KC - 1))
                    mm.then_inc(projected, 1)

            def aggregate(s, par, c):
                b = s - 1
                n = b * T + c
                if c == 0:
                    need(pe, xs_ready, (b + 1) * T)
                need(pe, at_tile_ready, n + 1)
                need(pe, hp_ready, n - 1)
                for j in range(T):
                    for part in range(2):
                        for g in range(2):
                            mm = pe.matmul(ps_agg[c % 2][:, g, 0:Q * C], at_tile[c % 2][:, j, :],
                                           xs[1 - par][:, j, part, g * Q:(g + 1) * Q, :],
                                           start=(j == 0 and part == 0), stop=(j == T - 1 and part == 1))
                mm.then_inc(aggregated, 1)

            walk(pe, {"P": project, "A": aggregate})


def layer1(nc, x1_d, at_d, W, a1, a2, out, B):
    N, D = x1_d.shape[1], x1_d.shape[2]
    H, _, d = W.shape
    T = N // P
    TH = T // 2
    NH = N // 2
    KC = D // P
    C = d + 2
    Q = H // 2
    U = 2 * H
    assert H * d == D and U == 16 and T == 8

    with ExitStack() as ctx:
        sb = lambda name, shape, dt: ctx.enter_context(nc.sbuf_tensor("l1_" + name, shape, dt))
        ps = lambda name, shape, dt: ctx.enter_context(nc.psum_tensor("l1_" + name, shape, dt))
        sem = lambda name: ctx.enter_context(nc.semaphore("l1_" + name))

        at_half = [sb(f"at_half{i}", [P, T, NH], U8) for i in range(2)]
        at_tile = [sb(f"at_tile{i}", [P, T, P], F32R) for i in range(2)]
        gate = [sb(f"gate{i}", [P, T, NH], F32R) for i in range(2)]
        xs = [sb(f"xs{i}", [P, T, Q, 4, C], F32R) for i in range(2)]
        hh = sb("hh", [P, T, H, C], F32)
        xw = sb("xw", [P, T, 2, C], F32)
        x_in = sb("x_in", [P, D], F32)
        x_res = [sb(f"x_res{i}", [P, D], F32) for i in range(TH)]
        xT_hi = [sb(f"xT_hi{i}", [P, KC, P], F32R) for i in range(2)]
        xT_lo = sb("xT_lo", [P, KC, P], F32R)
        w_hi = sb("w_hi", [P, KC, D], F32R)
        w_lo = sb("w_lo", [P, KC, D], F32R)
        wa = sb("wa", [P, KC, 2 * H], F32)
        wa_s = sb("wa_s", [P, KC, 4 * H], F32R)
        s_low = sb("s_low", [P, 2 * H], F32)
        s_cols = sb("s_cols", [P, (T - 1) * 48 + P], F32)
        s_rows = [sb(f"s_rows{i}", [P, NH], F32R) for i in range(2)]
        pick = sb("pick", [P, H, P], F32R)
        s2_max = sb("s2_max", [P, H], F32)
        s2_top = sb("s2_top", [P, H], F32)
        s2_sh = sb("s2_sh", [P, T, H], F32)
        z = sb("z", [P, T, H], F32)
        zmin = sb("zmin", [P, 2, T, H], F32)
        p12 = sb("p12", [P, T, 2, H], F32)
        nxt = sb("nxt", [P, 4, T, H], F32)
        cur_v = sb("cur_v", [P, T, H], F32)
        cur_a = sb("cur_a", [P, 3, T, H], F32)
        ev = [sb(f"ev{i}", [P, TH, 4, C], F32) for i in range(2)]
        ax = [sb(f"ax{i}", [P, TH, Q, C], F32) for i in range(2)]
        rden = sb("rden", [P, TH], F32)
        y = sb("y", [P, TH, D], F32)
        stats = [sb(f"stats{i}", [P, 6], F32) for i in range(2)]
        mv = [sb(f"mv{i}", [P, 2], F32) for i in range(2)]
        rstd = [sb(f"rstd{i}", [P, 1], F32) for i in range(2)]
        mhalf = sb("mhalf", [P, 1], F32)
        ident = sb("ident", [P, P], F32)
        hh_flat = hh[:, :, :, :].rearrange("p t h c -> p (t h c)")
        w_raw = hh_flat[:, 0:KC * D].rearrange("p (k n) -> p k n", k=KC)
        prod = hh_flat[:, KC * D:2 * KC * D].rearrange("p (k n) -> p k n", k=KC)
        a_bc = y[:, 0:2, :]
        pick_raw = y[:, 2:4, :].rearrange("p a (h m) -> p (a h) m", m=P)

        ps_xt = ps("ps_xt", [P, KC, P], F32)
        ps_y = ps("ps_y", [P, D], F32)
        ps_s = ps("ps_s", [P, 512], F32)
        ps_b = [ps(f"ps_b{i}", [P, NH], F32) for i in range(2)]
        ps_o = [ps(f"ps_o{i}", [P, 512], F32) for i in range(2)]
        ps_ax = ps("ps_ax", [P, 512], F32)

        w_loaded = sem("w_loaded")
        a_loaded = sem("a_loaded")
        prod_ready = sem("prod_ready")
        wa_ready = sem("wa_ready")
        hi_ready = sem("hi_ready")
        w_ready = sem("w_ready")
        const_ready = sem("const_ready")
        ident_ready = sem("ident_ready")
        sp_passed = sem("sp_passed")
        pool_passed = sem("pool_passed")
        dve_passed = sem("dve_passed")
        pick_raw_ready = sem("pick_raw_ready")
        pick_ready = sem("pick_ready")
        at_loaded = [sem(f"at_loaded{i}") for i in range(2)]
        at_tile_ready = sem("at_tile_ready")
        x_loaded = sem("x_loaded")
        x_res_loaded = [sem(f"x_res_loaded{i}") for i in range(TH)]
        x_turned = sem("x_turned")
        xT_hi_ready = sem("xT_hi_ready")
        xT_lo_ready = sem("xT_lo_ready")
        projected = sem("projected")
        s_low_ready = sem("s_low_ready")
        hh_ready = sem("hh_ready")
        s_ready = sem("s_ready")
        s_turned = sem("s_turned")
        rows_hi_ready = sem("rows_hi_ready")
        rows_ready = sem("rows_ready")
        s2_max_ready = sem("s2_max_ready")
        s2_top_ready = sem("s2_top_ready")
        shift_ready = sem("shift_ready")
        zmin_ready = sem("zmin_ready")
        p12_ready = sem("p12_ready")
        factors_ready = sem("factors_ready")
        nxt_ready = sem("nxt_ready")
        cur_v_ready = sem("cur_v_ready")
        cur_a_ready = sem("cur_a_ready")
        xw_ready = sem("xw_ready")
        xs_hi_ready = sem("xs_hi_ready")
        xs_ready = sem("xs_ready")
        spread = sem("spread")
        gate_ready = sem("gate_ready")
        gated = sem("gated")
        ev_ready = sem("ev_ready")
        ev2_ready = sem("ev2_ready")
        ax_done = sem("ax_done")
        ax_ready = sem("ax_ready")
        tot_ready = sem("tot_ready")
        tot2_ready = sem("tot2_ready")
        rden_ready = sem("rden_ready")
        y_ready = sem("y_ready")
        y2_ready = sem("y2_ready")
        stats_ready = sem("stats_ready")
        mv_ready = sem("mv_ready")
        var_ready = sem("var_ready")
        rstd_ready = sem("rstd_ready")
        out_ready = sem("out_ready")
        stored = [sem(f"stored{i}") for i in range(TH)]

        ORDER = []
        G_FIRST = {0: 0, 1: 2, 4: 5, 5: 7, **{j - 2: j for j in range(8, U)}}
        G_LAST = {0: 1, 1: 3, 3: 4, 4: 6}
        for n in range(U):
            if n == 0:
                ORDER += [("A", 1, 0), ("K", 0, 0), ("B", 0, 0)]
            if 2 <= n <= 10:
                ORDER.append(("P", n - 2, 1))
            if n == 1:
                ORDER.append(("R", 1, 0))
            if n == 12:
                ORDER.append(("R", 0, 1))
            if n in G_FIRST:
                ORDER.append(("G", G_FIRST[n], 0))
            if n + 1 < U:
                ORDER.append(("B", n + 1, 0))
            ORDER.append(("u", n, 0))
            if n == 11:
                ORDER.append(("z", 0, 1))
            ORDER.append(("C", (n - 2) % U, 0 if n >= 2 else -1))
            ORDER.append(("U", n, 0))
            if n == 11:
                ORDER.append(("M", 0, 1))
            for j in (G_LAST.get(n - 1), G_FIRST.get(n)):
                if j is not None and j + 2 < U:
                    ORDER.append(("T", j + 2, 0))
            if n >= 14:
                ORDER.append(("T", n - 14, 1))
            ORDER.append(("E", n, 0))
            if n in G_LAST:
                ORDER.append(("G", G_LAST[n], 0))
            if n < Q:
                ORDER.append(("x", Q + n, 0))
            if n >= 12:
                ORDER.append(("x", n - 12, 1))
            if 2 <= n <= 10:
                ORDER.append(("p", n - 2, 1))
            if n == 1:
                ORDER += [("r", 1, 0), ("Y", 1, -1)]
            if n == 12:
                ORDER.append(("r", 0, 1))
            if n == 10:
                ORDER.append(("m", 0, 1))
            ORDER.append(("c", (n - 1) % U, 0 if n >= 1 else -1))
            if n < Q - 1:
                ORDER += [("w", Q + 1 + n, 0), ("X", Q + 1 + n, 0)]
            if n >= 11:
                ORDER += [("w", n - 11, 1), ("X", n - 11, 1)]
            if n == 9:
                ORDER += [("A", 0, 1), ("Y", 0, 0)]
            if 2 <= n < 7:
                ORDER.append(("L", 5 + n - 2, -1))
            if 10 <= n < 15:
                ORDER.append(("L", n - 10, 0))

        def walk(eng, parts):
            def step(s, batches):
                for kind, k, db in ORDER:
                    if kind in parts and db in batches:
                        parts[kind](s + db, k)
            step(-1, (1,))
            step(0, (0, 1))
            with eng.Fori(1, B - 1) as s:
                step(s, (-1, 0, 1))
            step(B - 1, (-1, 0))
            step(B, (-1,))

        block = ctx.enter_context(nc.Block())

        @block.sync
        def _(sp):
            for k in range(KC):
                sp.dma_start(w_raw[:, k, :].rearrange("p (h o) -> p h o", h=H),
                             W[:, k * P:(k + 1) * P, :].rearrange("h p o -> p h o")).then_inc(w_loaded, 16)
            for i, a in enumerate((a1, a2)):
                sp.dma_start(a_bc[:, i, :], a.rearrange("h (o z) -> z (h o)", z=1).broadcast_to([P, D])).then_inc(a_loaded, 16)

            def load_at(b, half):
                need_first(sp, gate_ready, (b - 1) * U + (half + 1) * H, sp_passed)
                need_first(sp, at_tile_ready, (b - 1) * T * 2 + (half + 1) * T, sp_passed)
                sp.dma_start(at_half[half][:, :, :], at_d[bass.ds(b, 1), :, half * NH:(half + 1) * NH].rearrange(
                    "a (t p) n -> p (a t) n", p=P)).then_inc(at_loaded[half], 16)

            def load_x(b, t):
                if t < T:
                    need_first(sp, x_turned, b * T + t, sp_passed)
                    sp.dma_start(x_in[:, :], x1_d[bass.ds(b, 1), t * P:(t + 1) * P, :].rearrange("a p f -> (a p) f")
                                 ).then_inc(x_loaded, 16)

            def load_residual(b, half):
                for i in range(TH):
                    need_first(sp, stored[i], (b * 2 + half) * 16, sp_passed)
                    r = half * TH + i
                    sp.dma_start(x_res[i][:, :], x1_d[bass.ds(b, 1), r * P:(r + 1) * P, :].rearrange("a p f -> (a p) f")
                                 ).then_inc(x_res_loaded[i], 16)

            def store(b, k):
                half, i = divmod(k, 5)
                if i >= 1:
                    j = i - 1
                    r = half * TH + j
                    need_first(sp, out_ready, b * T + r + 1, sp_passed)
                    sp.dma_start(out[bass.ds(b, 1), r * P:(r + 1) * P, :].rearrange("a p f -> (a p) f"),
                                 x_res[j][:, :]).then_inc(stored[j], 16)

            walk(sp, {"A": load_at, "P": load_x, "Y": load_residual, "L": store})
            for i in range(TH):
                sp.wait_ge(stored[i], 16 * B * 2)

        @block.gpsimd
        def _(pool):
            pool.memset(ident[:, :], 0.0).then_inc(ident_ready, 1)
            pool.memset(pick_raw, 0.0).then_inc(pick_raw_ready, 1)
            pool.memset(mhalf[:, :], -0.5).then_inc(const_ready, 1)
            pool.memset(s_cols[:, :], 0.0).then_inc(const_ready, 1)
            pool.wait_ge(ident_ready, 1)
            pool.affine_select(out=ident[:, :], in_=ident[:, :], compare_op=ALU.not_equal, fill=1.0, base=0,
                               pattern=[[-1, P]], channel_multiplier=1).then_inc(ident_ready, 1)
            for base in range(2):
                pool.wait_ge(pick_raw_ready, base + 1)
                pool.affine_select(out=pick_raw, in_=pick_raw, compare_op=ALU.not_equal, fill=1.0, base=-32 * base,
                                   pattern=[[-1, H], [0, P]], channel_multiplier=1).then_inc(pick_raw_ready, 1)
            pool.wait_ge(w_ready, 2)
            pool.memset(hh[:, :, :, d:d + 1], 1.0).then_inc(const_ready, 1)
            pool.memset(hh[:, :, :, d + 1:C], 0.0).then_inc(const_ready, 1)
            pool.wait_ge(const_ready, 4)

            def tile(b, j):
                half, i = j // T, j % TH
                if j % T == 0:
                    need_first(pool, at_loaded[half], (b + 1) * 16, pool_passed)
                need_first(pool, ax_done, b * U + j - 1, pool_passed)
                pool.tensor_scalar(at_tile[i % 2][:, :, :], at_half[half][:, :, i * P:(i + 1) * P], 1.0, 0.0,
                                   ALU.mult, ALU.add).then_inc(at_tile_ready, 1)

            def weigh(b, h):
                n = b * H + h
                if h == 0:
                    need(pool, hh_ready, (b + 1) * T)
                    need(pool, p12_ready, (b + 1) * 2)
                need(pool, xs_ready, n)
                pool.tensor_tensor(xw[:, :, :, :], hh[:, :, h, :].unsqueeze(2).broadcast_to([P, T, 2, C]),
                                   p12[:, :, :, h].unsqueeze(3).broadcast_to([P, T, 2, C]), ALU.mult
                                   ).then_inc(xw_ready, 1)

            def split_low(b, h):
                q, i = divmod(h, Q)
                need(pool, xs_hi_ready, b * H + h + 1)
                pool.tensor_tensor(xs[q][:, :, i, 1:4:2, :], xw[:, :, :, :],
                                  xs[q][:, :, i, 0:4:2, :].bitcast(F32), ALU.subtract).then_inc(xs_ready, 1)

            def combine(b, n):
                m = b * U + n
                need(pool, ev_ready, (m + 1) * TH)
                pool.tensor_tensor(ev[n % 2][:, :, 0:2, :], ev[n % 2][:, :, 0:2, :], ev[n % 2][:, :, 2:4, :], ALU.add
                                   ).then_inc(ev2_ready, 1)
                need(pool, ev2_ready, m + 1)
                pool.tensor_tensor(ev[n % 2][:, :, 2, :], ev[n % 2][:, :, 0, :], ev[n % 2][:, :, 1, :], ALU.add
                                   ).then_inc(tot_ready, 1)

            def top(b, _):
                need(pool, s2_max_ready, b + 1)
                need_first(pool, shift_ready, b, pool_passed)
                pool.partition_all_reduce(s2_top[:, :], s2_max[:, :], P, bass.bass_isa.ReduceOp.max
                                          ).then_inc(s2_top_ready, 1)

            def norm(b, k):
                half, j = divmod(k, 5)
                if j < TH:
                    n = b * T + half * TH + j + 1
                    need_first(pool, mv_ready, n, pool_passed)
                    pool.tensor_scalar(mv[j % 2][:, 1:2], mv[j % 2][:, 1:2], EPS, 1.0, ALU.add, ALU.mult
                                       ).then_inc(var_ready, 1)
                    need(pool, var_ready, n)
                    pool.tensor_tensor(rstd[j % 2][:, :], mv[j % 2][:, 1:2], mhalf[:, :], ALU.pow
                                       ).then_inc(rstd_ready, 1)

            walk(pool, {"T": tile, "w": weigh, "x": split_low, "c": combine, "m": top, "L": norm})

        @block.scalar
        def _(act):
            act.wait_ge(w_loaded, 16 * KC)
            act.activation(w_hi[:, :, :], w_raw, ACT.Copy).then_inc(hi_ready, 1)
            act.wait_ge(wa_ready, 2)
            act.activation(wa_s[:, :, 0:2 * H], wa[:, :, :], ACT.Copy).then_inc(hi_ready, 1)
            act.wait_ge(pick_raw_ready, 3)
            act.activation(pick[:, :, :], pick_raw, ACT.Copy).then_inc(pick_ready, 1)
            act.wait_ge(const_ready, 4)

            def project(b, t):
                n = b * T + t
                if t < T:
                    need(act, x_turned, n + 1)
                    need(act, projected, n - 1)
                    act.activation(xT_hi[t % 2][:, :, :], ps_xt[:, :, :], ACT.Copy).then_inc(xT_hi_ready, 1)
                if t >= 1:
                    j = t - 1
                    m = b * T + j
                    need(act, projected, m + 1)
                    need(act, s_ready, m)
                    act.activation(s_low[:, :], ps_s[:, 2 * H:4 * H], ACT.Copy).then_inc(s_low_ready, 1)
                    if j == 0:
                        need(act, xw_ready, b * H)
                    act.activation(hh[:, j, :, 0:d], ps_y[:, :].rearrange("p (h o) -> p h o", h=H), ACT.Copy
                                   ).then_inc(hh_ready, 1)

            def rows(b, half):
                m = b * 2 + half
                need(act, s_turned, m + 1)
                need(act, spread, (b - 1) * U + (half + 1) * H)
                act.activation(s_rows[half][:, :], ps_xt[:, :, :].rearrange("p t n -> p (t n)"), ACT.Copy
                               ).then_inc(rows_hi_ready, 1)

            def weights(b, _):
                need(act, shift_ready, b + 1)
                need(act, xw_ready, b * H)
                act.activation(p12[:, :, 0, :], s2_sh[:, :, :], ACT.Exp).then_inc(p12_ready, 1)
                act.activation(p12[:, :, 1, :], s2_sh[:, :, :], ACT.Exp, scale=SLOPE).then_inc(p12_ready, 1)
                need(act, zmin_ready, (b + 1) * 2)
                need(act, cur_v_ready, b)
                act.activation(nxt[:, 3, :, :], zmin[:, 1, :, :], ACT.Exp).then_inc(factors_ready, 1)
                act.activation(nxt[:, 1, :, :], zmin[:, 0, :, :], ACT.Exp).then_inc(factors_ready, 1)

            def take(b, _):
                need(act, ax_ready, b * 4 * TH)
                need(act, ev_ready, b * U * TH)
                need(act, nxt_ready, b + 1)
                act.activation(cur_a[:, :, :, :], nxt[:, 1:4, :, :], ACT.Copy).then_inc(cur_a_ready, 1)
                act.wait_ge(cur_a_ready, b + 1)

            def split(b, h):
                q, i = divmod(h, Q)
                need(act, xw_ready, b * H + h + 1)
                need(act, gated, ((b - 1) * U + H + h + 1) * TH)
                if i == 0:
                    need(act, ax_done, (b - 1) * U + H + (q + 1) * Q)
                act.activation(xs[q][:, :, i, 0:4:2, :], xw[:, :, :, :], ACT.Copy).then_inc(xs_hi_ready, 1)

            def unit(b, n):
                half, h = divmod(n, H)
                for i in range(TH):
                    m = (b * U + n) * TH + i
                    t = half * TH + i
                    need(act, gated, m + 1)
                    if i == 0:
                        need(act, y_ready, b * U + n - 1)
                    act.activation(ev[n % 2][:, i, 0:2, :], ps_o[i % 2][:, 0:2 * C].rearrange("p (a c) -> p a c", a=2),
                                   ACT.Copy, scale=cur_a[:, 0, t, h:h + 1])
                    act.activation(ev[n % 2][:, i, 2:4, :], ps_o[i % 2][:, 2 * C:4 * C].rearrange("p (a c) -> p a c", a=2),
                                   ACT.Copy, scale=cur_a[:, 1, t, h:h + 1]).then_inc(ev_ready, 1)

            def adj_part(b, k):
                g, i = divmod(k, TH)
                half, q = divmod(g, 2)
                need(act, ax_done, b * U + k + 1)
                if i == 0:
                    need(act, y_ready, b * U + (g - 1) * Q)
                for j in range(Q):
                    ins = act.activation(ax[g % 2][:, i, j, :], ps_ax[:, j * C:(j + 1) * C], ACT.Copy,
                                         scale=cur_a[:, 2, half * TH + i, q * Q + j:q * Q + j + 1])
                ins.then_inc(ax_ready, 1)

            walk(act, {"G": adj_part, "P": project, "R": rows, "M": weights, "K": take, "X": split, "E": unit})

        @block.vector
        def _(dve):
            dve.wait_ge(w_loaded, 16 * KC)
            dve.wait_ge(a_loaded, 32)
            for i in range(2):
                if i:
                    dve.wait_ge(wa_ready, i)
                dve.tensor_tensor(prod, w_raw, a_bc[:, i, :].unsqueeze(1).broadcast_to([P, KC, D]), ALU.mult
                                  ).then_inc(prod_ready, 1)
                dve.wait_ge(prod_ready, i + 1)
                for k in range(KC):
                    ins = dve.tensor_reduce(wa[:, k, i * H:(i + 1) * H], prod[:, k, :].rearrange("p (h o) -> p h o", h=H),
                                            AX.X, ALU.add)
                ins.then_inc(wa_ready, 1)
            dve.wait_ge(hi_ready, 2)
            dve.tensor_tensor(w_lo[:, :, :], w_raw, w_hi[:, :, :].bitcast(F32), ALU.subtract).then_inc(w_ready, 1)
            dve.tensor_tensor(wa_s[:, :, 2 * H:4 * H], wa[:, :, :], wa_s[:, :, 0:2 * H].bitcast(F32), ALU.subtract
                              ).then_inc(w_ready, 1)
            dve.wait_ge(const_ready, 4)
            dve.wait_ge(pick_ready, 1)
            dve.wait_ge(w_ready, 2)

            def project(b, t):
                n = b * T + t
                if t < T:
                    need(dve, xT_hi_ready, n + 1)
                    need(dve, projected, n)
                    dve.tensor_tensor(xT_lo[:, :, :], ps_xt[:, :, :], xT_hi[t % 2][:, :, :].bitcast(F32),
                                      ALU.subtract).then_inc(xT_lo_ready, 1)
                if t >= 1:
                    j = t - 1
                    need(dve, s_low_ready, b * T + j + 1)
                    if j == 0:
                        need(dve, s_turned, b * 2)
                    dve.tensor_tensor(s_cols[:, j * 48:j * 48 + H], ps_s[:, 0:H], s_low[:, 0:H], ALU.add)
                    dve.tensor_tensor(s_cols[:, j * 48 + 32:j * 48 + 48], ps_s[:, 0:2 * H], s_low[:, :], ALU.add
                                      ).then_inc(s_ready, 1)

            def rows(b, half):
                m = b * 2 + half
                need(dve, rows_hi_ready, m + 1)
                lo = slice(32, 32 + H)
                dve.tensor_tensor(s_rows[half][lo, :], ps_xt[lo, :, :].rearrange("p t n -> p (t n)"),
                                  s_rows[half][lo, :].bitcast(F32), ALU.subtract).then_inc(rows_ready, 1)

            def top(b, _):
                by_tile = s_cols[:, 0:T * 48].rearrange("p (t c) -> p t c", t=T)
                s2 = by_tile[:, :, 32 + H:48]
                need(dve, s_ready, (b + 1) * T)
                dve.tensor_reduce(s2_max[:, :], s2.rearrange("p t h -> p h t"), AX.X, ALU.max).then_inc(s2_max_ready, 1)

            def exponents(b, _):
                by_tile = s_cols[:, 0:T * 48].rearrange("p (t c) -> p t c", t=T)
                s1 = by_tile[:, :, 32:32 + H]
                s2 = by_tile[:, :, 32 + H:48]
                need(dve, s2_top_ready, b + 1)
                top_bc = s2_top[:, :].unsqueeze(1).broadcast_to([P, T, H])
                need(dve, factors_ready, b * 2)
                dve.tensor_tensor(z[:, :, :], s1, top_bc, ALU.add)
                dve.tensor_tensor(s2_sh[:, :, :], s2, top_bc, ALU.subtract).then_inc(shift_ready, 1)
                need(dve, shift_ready, b + 1)
                dve.tensor_scalar(zmin[:, 0, :, :], z[:, :, :], 1.0 - SLOPE, 0.0, ALU.mult, ALU.min).then_inc(zmin_ready, 1)
                dve.tensor_scalar(zmin[:, 1, :, :], z[:, :, :], SLOPE - 1.0, 0.0, ALU.mult, ALU.min).then_inc(zmin_ready, 1)
                need(dve, cur_a_ready, b)
                dve.tensor_scalar(nxt[:, 0, :, :], s2, -1.0, None, ALU.mult)

            def factors(b, _):
                need(dve, factors_ready, (b + 1) * 2)
                dve.tensor_scalar(nxt[:, 2, :, :], nxt[:, 3, :, :], -1.0, None, ALU.mult).then_inc(nxt_ready, 1)

            def take(b, _):
                need(dve, gate_ready, b * U)
                need(dve, nxt_ready, b + 1)
                dve.tensor_copy(cur_v[:, :, :], nxt[:, 0, :, :]).then_inc(cur_v_ready, 1)
                dve.wait_ge(cur_v_ready, b + 1)

            def unit_start(b, n):
                half, h = divmod(n, H)
                m = b * U + n
                if h == 0:
                    need(dve, at_loaded[half], (b + 1) * 16)
                need(dve, spread, m + 1)
                need(dve, gated, (m - 1) * TH)
                for u in range(T // 2):
                    dve.scalar_tensor_tensor(out=gate[n % 2][:, u, :], in0=ps_b[n % 2][:, :],
                                             scalar=cur_v[:, u, h:h + 1], in1=at_half[half][:, u, :],
                                             op0=ALU.is_gt, op1=ALU.mult)

            def unit(b, n):
                half, h = divmod(n, H)
                for u in range(T // 2, T):
                    ins = dve.scalar_tensor_tensor(out=gate[n % 2][:, u, :], in0=ps_b[n % 2][:, :],
                                                   scalar=cur_v[:, u, h:h + 1], in1=at_half[half][:, u, :],
                                                   op0=ALU.is_gt, op1=ALU.mult)
                ins.then_inc(gate_ready, 1)

            def combine(b, n):
                half, h = divmod(n, H)
                m = b * U + n
                g = n // Q
                e = ev[n % 2]
                need(dve, ax_ready, (b * 4 + g + 1) * TH)
                need(dve, tot_ready, m + 1)
                dve.tensor_tensor(e[:, :, 3, :], e[:, :, 2, :], ax[g % 2][:, :, h % Q, :], ALU.add).then_inc(tot2_ready, 1)
                need(dve, tot2_ready, m + 1)
                dve.reciprocal(rden[:, :], e[:, :, 3, d]).then_inc(rden_ready, 1)
                need(dve, rden_ready, m + 1)
                if h == 0:
                    need(dve, y2_ready, b * T + half * TH)
                dve.tensor_tensor(y[:, :, h * d:(h + 1) * d], e[:, :, 3, 0:d],
                                  rden[:, :].unsqueeze(2).broadcast_to([P, TH, d]), ALU.mult).then_inc(y_ready, 1)

            def residual(b, half):
                need(dve, y_ready, b * U + (half + 1) * H)
                for i in range(TH):
                    need(dve, x_res_loaded[i], (b * 2 + half + 1) * 16)
                    dve.tensor_tensor(x_res[i][:, :], y[:, i, :], x_res[i][:, :], ALU.add).then_inc(y2_ready, 1)

            def norm(b, k):
                half, i = divmod(k, 5)
                if i < TH:
                    n = b * T + half * TH + i + 1
                    need(dve, y2_ready, n)
                    dve.bn_stats(stats[i % 2][:, :], x_res[i][:, :]).then_inc(stats_ready, 1)
                    need_first(dve, stats_ready, n, dve_passed)
                    dve.bn_aggr(mv[i % 2][:, :], stats[i % 2][:, :]).then_inc(mv_ready, 1)
                if i >= 1:
                    j = i - 1
                    need(dve, rstd_ready, b * T + half * TH + j + 1)
                    dve.tensor_scalar(x_res[j][:, :], x_res[j][:, :], mv[j % 2][:, 0:1], rstd[j % 2][:, 0:1],
                                      ALU.subtract, ALU.mult).then_inc(out_ready, 1)

            walk(dve, {"p": project, "r": rows, "m": top, "z": exponents, "M": factors, "K": take, "u": unit_start,
                       "U": unit, "C": combine, "Y": residual, "L": norm})

        @block.tensor
        def _(pe):
            pe.wait_ge(ident_ready, 2)
            pe.wait_ge(w_ready, 2)
            pe.wait_ge(pick_ready, 1)
            pe.wait_ge(const_ready, 4)

            def project(b, t):
                n = b * T + t
                if t < T:
                    need(pe, x_loaded, (n + 1) * 16)
                    need(pe, xT_lo_ready, n)
                    if t == 0:
                        need(pe, rows_ready, b * 2)
                    for k in range(KC):
                        mm = pe.transpose(ps_xt[:, k, :], x_in[:, k * P:(k + 1) * P], ident[:, :])
                    mm.then_inc(x_turned, 1)
                if t >= 1:
                    j = t - 1
                    m = b * T + j
                    need(pe, xT_lo_ready, m + 1)
                    need(pe, hh_ready, m)
                    need(pe, s_ready, m)
                    hi, lo = xT_hi[j % 2], xT_lo
                    for k in range(KC):
                        first, last = k == 0, k == KC - 1
                        pe.matmul(ps_y[:, :], hi[:, k, :], w_hi[:, k, :], start=first, stop=False)
                        pe.matmul(ps_y[:, :], hi[:, k, :], w_lo[:, k, :], start=False, stop=False)
                        pe.matmul(ps_s[:, 0:4 * H], hi[:, k, :], wa_s[:, k, :], start=first, stop=False)
                        pe.matmul(ps_y[:, :], lo[:, k, :], w_hi[:, k, :], start=False, stop=last)
                        mm = pe.matmul(ps_s[:, 0:4 * H], lo[:, k, :], wa_s[:, k, :], start=False, stop=last)
                    mm.then_inc(projected, 1)

            def rows(b, half):
                if half == 0:
                    need(pe, s_ready, (b + 1) * T)
                    need(pe, xT_lo_ready, (b + 1) * T)
                need(pe, rows_ready, b * 2 + half)
                for i in range(TH):
                    mm = pe.transpose(ps_xt[:, i, :], s_cols[:, (half * TH + i) * 48:(half * TH + i) * 48 + P], ident[:, :])
                mm.then_inc(s_turned, 1)

            def spread_scores(b, n):
                half, h = divmod(n, H)
                m = b * U + n
                if h == 0:
                    need(pe, rows_ready, b * 2 + half + 1)
                need(pe, gate_ready, m - 1)
                pe.matmul(ps_b[n % 2][:, :], pick[:, h, :], s_rows[half][:, :], start=True, stop=True).then_inc(spread, 1)

            def adj_part(b, k):
                g, i = divmod(k, TH)
                q = g % 2
                if k in (0, Q):
                    need(pe, xs_ready, b * H + (q + 1) * Q)
                need(pe, at_tile_ready, b * U + k + 1)
                need(pe, ax_ready, b * U + k)
                for u in range(T):
                    for part in range(2):
                        mm = pe.matmul(ps_ax[:, 0:Q * C], at_tile[i % 2][:, u, :], xs[q][:, u, :, 2 + part, :],
                                       start=(u == 0 and part == 0), stop=(u == T - 1 and part == 1))
                mm.then_inc(ax_done, 1)

            def unit(b, n):
                half, h = divmod(n, H)
                q, e = divmod(h, Q)
                need(pe, gate_ready, b * U + n + 1)
                for i in range(TH):
                    m = (b * U + n) * TH + i
                    need(pe, ev_ready, m - 1)
                    for u in range(T):
                        mm = pe.matmul(ps_o[i % 2][:, 0:4 * C], gate[n % 2][:, u, i * P:(i + 1) * P],
                                       xs[q][:, u, e, :, :].rearrange("p a c -> p (a c)"), start=(u == 0), stop=(u == T - 1))
                    mm.then_inc(gated, 1)

            walk(pe, {"P": project, "R": rows, "B": spread_scores, "G": adj_part, "U": unit})


_INS = ["x", "adj", "L0_gnn_W_l", "L0_gnn_W_r", "L0_gnn_a", "L1_gnn_W", "L1_gnn_a1", "L1_gnn_a2"]


def program(nc, x, adj, W_l, W_r, a, W, a1, a2, out):
    B, N, D = x.shape
    at_d = nc.dram_tensor("at_scratch", [B, N, N], U8, kind="Internal").ap()
    x1_d = nc.dram_tensor("x1_scratch", [B, N, D], F32, kind="Internal").ap()
    layer0(nc, x, adj, W_r, a, x1_d, at_d, B)
    layer1(nc, x1_d, at_d, W, a1, a2, out, B)


def kernel(**inputs):
    import numpy as _np
    import concourse.bacc as _bacc
    from concourse import mybir as _mybir
    from concourse.bass_utils import run_bass_kernel_spmd as _run

    nc = _bacc.Bacc("TRN2", target_bir_lowering=False, num_devices=1)
    arrays, args = {}, []
    for name in _INS:
        arr = _np.ascontiguousarray(inputs[name])
        arrays[f"in_{name}_dram"] = arr
        args.append(nc.dram_tensor(f"in_{name}_dram", arr.shape, _mybir.dt.from_np(arr.dtype), kind="ExternalInput").ap())
    args.append(nc.dram_tensor("out_0_dram", tuple(inputs["x"].shape), _mybir.dt.float32, kind="ExternalOutput").ap())
    program(nc, *args)
    r = _run(nc, [arrays], core_ids=[0])
    return r.results[0]["out_0_dram"]
```
